# Optimizing a Trainium2 kernel written in Bass

```python
import numpy as np
import jax
import jax.numpy as jnp

def _softmax(x, axis=-1):
    return jax.nn.softmax(x, axis=axis)

def _gelu(x):
    return jax.nn.gelu(x, approximate=True)

def _silu(x):
    return jax.nn.silu(x)

def _sigmoid(x):
    return jax.nn.sigmoid(x)

def _layernorm(x, axis=-1, eps=1e-05):
    m = jnp.mean(x, axis=axis, keepdims=True)
    v = jnp.var(x, axis=axis, keepdims=True)
    return (x - m) / jnp.sqrt(v + eps)

def _scatter_add(tgt, idx, src, axis=0):
    return tgt.at[idx].add(src)

def _segment_sum(src, seg, n):
    return jax.ops.segment_sum(src, seg, n)
kernel_name = 'mk_gnn_resnorm_d1_gnn_r8_c1f8e8'

def setup_inputs(seed: int=0):
    np.random.seed(seed)
    _w = jnp.asarray

    def _rec_inputs():
        import jax
        import jax.numpy as jnp
        _gk = jax.random.key(seed)
        x = -0.0005121 + 1.001 * jax.random.normal(jax.random.fold_in(_gk, 1), (12500, 64), jnp.float32)
        src = jax.random.randint(jax.random.fold_in(_gk, 2), (200000,), 0, 12500, jnp.int32)
        dst = jax.random.randint(jax.random.fold_in(_gk, 3), (200000,), 0, 12500, jnp.int32)
        _o = jnp.argsort(dst, stable=True)
        src = src[_o]
        dst = dst[_o]
        edge_type_64 = jax.random.randint(jax.random.fold_in(_gk, 12), (200000,), 0, 64, jnp.int32)
        return (x, src, dst, edge_type_64)
    x, src, dst, edge_type_64 = _rec_inputs()

    def _L0_gnn_setup():
        import jax, jax.numpy as jnp
        import numpy as np
        N_NODES = 6250
        N_EDGES = 50000
        IN_DIM = 64
        OUT_DIM = 64
        NUM_RELS = 64
        NUM_BASES = 8
        key = jax.random.key(seed)
        k = jax.random.split(key, 8)
        node_feat = jax.random.normal(k[0], (N_NODES, IN_DIM), dtype=jnp.float32)
        src = jax.random.randint(k[1], (N_EDGES,), 0, N_NODES, dtype=jnp.int32)
        dst = jax.random.randint(k[2], (N_EDGES,), 0, N_NODES, dtype=jnp.int32)
        edge_type = jax.random.randint(k[3], (N_EDGES,), 0, NUM_RELS, dtype=jnp.int32)
        bound = 1.0 / np.sqrt(IN_DIM)
        weight = jax.random.uniform(k[4], (NUM_BASES, IN_DIM, OUT_DIM), dtype=jnp.float32, minval=-bound, maxval=bound)
        w_comp = jax.random.uniform(k[5], (NUM_RELS, NUM_BASES), dtype=jnp.float32, minval=-bound, maxval=bound)
        loop_weight = jax.random.uniform(k[6], (IN_DIM, OUT_DIM), dtype=jnp.float32, minval=-bound, maxval=bound)
        bias = jnp.zeros((OUT_DIM,), dtype=jnp.float32)
        return {'node_feat': node_feat, 'weight': weight, 'w_comp': w_comp, 'loop_weight': loop_weight, 'bias': bias, 'src': src, 'dst': dst, 'edge_type': edge_type}
    _L0_gnn_all = _L0_gnn_setup()
    _L0_gnn_in = {k: v for k, v in _L0_gnn_all.items() if k in ('weight', 'w_comp', 'loop_weight', 'bias')}
    del _L0_gnn_all
    return {'x': x, 'src': src, 'dst': dst, 'edge_type_64': edge_type_64, 'L0_gnn_weight': _L0_gnn_in['weight'], 'L0_gnn_w_comp': _L0_gnn_in['w_comp'], 'L0_gnn_loop_weight': _L0_gnn_in['loop_weight'], 'L0_gnn_bias': _L0_gnn_in['bias']}

def reference(x, src, dst, edge_type_64, L0_gnn_weight, L0_gnn_w_comp, L0_gnn_loop_weight, L0_gnn_bias):
    import jax
    import jax.numpy as jnp

    def _L0_gnn_ref(node_feat, weight, w_comp, loop_weight, bias, src, dst, edge_type):
        import jax, jax.numpy as jnp
        import numpy as np
        N_NODES = 6250
        N_EDGES = 50000
        IN_DIM = 64
        OUT_DIM = 64
        NUM_RELS = 64
        NUM_BASES = 8
        N = node_feat.shape[0]
        in_deg = jax.ops.segment_sum(jnp.ones_like(dst, dtype=node_feat.dtype), dst, num_segments=N)
        in_norm = (1.0 / (in_deg + 1.0))[:, None]
        x_src = node_feat[src]
        xb = jnp.einsum('ei,bio->ebo', x_src, weight)
        coef = w_comp[edge_type]
        msg = jnp.einsum('ebo,eb->eo', xb, coef)
        msg = msg * in_norm[dst]
        agg = jax.ops.segment_sum(msg, dst, num_segments=N)
        loop_msg = node_feat @ loop_weight
        out = agg + loop_msg * in_norm + bias
        return jax.nn.relu(out)
    x = _layernorm(x + _L0_gnn_ref(x, L0_gnn_weight, L0_gnn_w_comp, L0_gnn_loop_weight, L0_gnn_bias, src, dst, edge_type_64), axis=-1)
    return x

_drawn_inputs = setup_inputs


def setup_inputs(seed=0):
    import zlib

    import numpy as np

    out = dict(_drawn_inputs(seed))
    spreads = {'L0_gnn_bias': (0.0, 0.1)}
    factors = {'L0_gnn_weight': 3.104, 'L0_gnn_w_comp': 3.139}
    for name, (base, spread) in spreads.items():
        noise = np.random.default_rng([zlib.crc32(name.encode()), seed]).standard_normal(out[name].shape)
        drawn = base * np.exp(spread * noise) if base else spread * noise
        out[name] = jnp.asarray(drawn.astype(out[name].dtype))
    for name, factor in factors.items():
        out[name] = (out[name] * factor).astype(out[name].dtype)
    return out
```

```python
import concourse.bass as bass
from concourse import mybir
from contextlib import ExitStack


def rgcn_kernel(nc, x, src, dst, etype, weight, w_comp, loop_w, bias, out):
    fp32, bf16, i32 = mybir.dt.float32, mybir.dt.bfloat16, mybir.dt.int32
    ALU, ACT, AX = mybir.AluOpType, mybir.ActivationFunctionType, mybir.AxisListType
    ds = bass.ds

    N, D = x.shape
    E = src.shape[0]
    NB = weight.shape[0]
    NT = w_comp.shape[0]
    P = 128
    D1 = D + 1
    B1 = NB + 1
    WIN = 14
    CQ = 4
    QR = 4
    CR = CQ * QR
    ER = P * CR
    NR = -(-E // ER)
    NC = -(-E // P)
    LAST = NR - 1
    EL = E - LAST * ER
    CL = NC - LAST * CR
    NBLK = -(-N // P)
    NPAD = NBLK * P
    SW = B1 * WIN
    FAR = 4096.0
    EPS = 1e-5
    LATE = 2
    assert NR == NBLK and CQ * SW <= 512 and NPAD >= N + WIN and NT * 2 == P

    def chunks_of(i, q):
        if isinstance(i, int) and i == LAST:
            return max(0, min(CQ, CL - CQ * q))
        return CQ

    ctx = ExitStack()
    with ctx:
        def sb(name, shape, dt):
            return ctx.enter_context(nc.sbuf_tensor(name, shape, dt))

        def pb(name, shape, dt=fp32):
            return ctx.enter_context(nc.psum_tensor(name, shape, dt))

        def sem(name):
            return ctx.enter_context(nc.semaphore(name))

        def sems(name, n=QR):
            return [sem(f"{name}{j}") for j in range(n)]

        src_nat = sb("src_nat", [NR, ER], i32)
        dst_nat = sb("dst_nat", [NR, ER], i32)
        typ_nat = sb("typ_nat", [NR, ER], i32)
        src_f = sb("src_f", [NR, ER], fp32)
        rel_f = sb("rel_f", [NR, ER], fp32)
        typ_b = sb("typ_b", [NR, ER], bf16)
        src_t = sb("src_t", [P, NR * CR], fp32)
        rel_t = sb("rel_t", [P, NR * CR], fp32)
        lo = sb("lo", [NR, CR], fp32)
        hi = sb("hi", [NR, CR], fp32)
        span = sb("span", [NR, CR], fp32)
        wide = sb("wide", [NR, CR], fp32)
        shift = sb("shift", [NR, CR], fp32)
        lo_i = sb("lo_i", [NR, CR], i32)
        base_row = sb("base_row", [1, NR * CR], i32)
        round_lo = sb("round_lo", [NR, 1], fp32)
        finished_to = sb("finished_to", [P, 1], fp32)
        odd = sb("odd", [NR, 2], fp32)
        odd_i = sb("odd_i", [1, 1], i32)
        iota_p = sb("iota_p", [P, 1], fp32)
        type_p = sb("type_p", [P, 1], fp32)
        type_hi = sb("type_hi", [P, 1], fp32)
        iota_w = sb("iota_w", [P, WIN], fp32)
        ident = sb("ident", [P, P], fp32)
        ident_b = sb("ident_b", [P, P], bf16)
        ones = sb("ones", [P, 1], fp32)
        eps = sb("eps", [P, 1], fp32)
        wc = sb("wc", [P, B1], fp32)
        wc_rest = sb("wc_rest", [P, B1], fp32)
        wc_low = sb("wc_low", [P, B1], fp32)
        wc_hi = sb("wc_hi", [P, B1], bf16)
        wc_a = sb("wc_a", [P, B1], bf16)
        wc_b = sb("wc_b", [P, B1], bf16)
        W = sb("W", [D1, B1, D1], fp32)
        loop_aug = sb("loop_aug", [D1, D1], fp32)
        acc_aug = sb("acc_aug", [D1, D1], fp32)
        idx = sb("idx", [P, QR, CQ], i32)
        xg = sb("xg", [P, QR, CQ, D1], fp32)
        type_1h = sb("type_1h", [P, 2, CQ * P], bf16)
        node_1h = sb("node_1h", [P, CR, WIN], fp32)
        S = sb("S", [P, QR, CQ * SW], fp32)
        Z = sb("Z", [D1, B1, CR * WIN], fp32)
        acc = sb("acc", [D1, NPAD], fp32)
        xb = sb("xb", [P, D], fp32)
        xbT = sb("xbT", [D1, P], fp32)
        accb = sb("accb", [D1, P], fp32)
        norm = sb("norm", [P, 1], fp32)
        deg1 = sb("deg1", [P, 1], fp32)
        h = sb("h", [P, D], fp32)
        y = sb("y", [P, D], fp32)
        stats = sb("stats", [P, 6], fp32)
        mv = sb("mv", [P, 2], fp32)
        std = sb("std", [P, 1], fp32)
        rstd = sb("rstd", [P, 1], fp32)
        ob = sb("ob", [P, D], fp32)
        g_idx_sb = sb("g_idx_sb", [P, 1], i32)
        g_x = sb("g_x", [P, D1], fp32)
        g_mask = sb("g_mask", [P, 1], fp32)
        g_cf = sb("g_cf", [P, B1], fp32)

        typ_ps = [pb(f"typ_ps{k}", [P, 512]) for k in range(2)]
        cf_ps = [pb(f"cf_ps{k}", [P, 512]) for k in range(2)]
        z_ps = [pb(f"z_ps{k}", [P, 512]) for k in range(2)]
        p_ps = pb("p_ps", [P, 512])
        f_ps = pb("f_ps", [P, 512])
        xbT_ps = f_ps[0:D, 0:P]
        fin_ps = f_ps[:, 256:256 + D1]

        def cf_slot(q):
            return cf_ps[q % 2][:, (q // 2) * 64:(q // 2) * 64 + CQ * B1].rearrange("p (c b) -> p c b", b=B1)

        src_in, dst_in, typ_in, w_in = sem("src_in"), sem("dst_in"), sem("typ_in"), sem("w_in")
        pads_set, wc_set, W_set = sem("pads_set"), sem("wc_set"), sem("W_set")
        base_in = sem("base_in")
        pool_const, dve_const = sem("pool_const"), sem("dve_const")
        src_cast, src_tr, src_out = sem("src_cast"), sem("src_tr"), sem("src_out")
        rel_set, rel_tr, rel_out = sem("rel_set"), sem("rel_tr"), sem("rel_out")
        typ_cast, lo_set, odd_set, odd_sum, odd_out = (
            sem("typ_cast"), sem("lo_set"), sem("odd_set"), sem("odd_sum"), sem("odd_out"))
        ident_cast, wc_split = sem("ident_cast"), sem("wc_split")
        step = sem("step")
        acc_zero, acc_zero_act, xg_one = sem("acc_zero"), sem("acc_zero_act"), sem("xg_one")
        idx_ready, gathered = sems("idx_ready"), sems("gathered")
        typ_spread, type_hot = sems("typ_spread"), sems("type_hot")
        cf_done, s_done, z_done, z_copied = sems("cf_done"), sems("s_done"), sems("z_done"), sems("z_copied")
        node_hot, projected, added = sem("node_hot"), sem("projected"), sem("added")
        x_in, stored = sem("x_in"), sem("stored")
        xbT_done, xbT_copied, accb_done, fin_done = sem("xbT_done"), sem("xbT_copied"), sem("accb_done"), sem("fin_done")
        deg1_done, norm_done, h_done, y_done = sem("deg1_done"), sem("norm_done"), sem("h_done"), sem("y_done")
        stats_done, mv_done, std_done, rstd_done, ob_done = (
            sem("stats_done"), sem("mv_done"), sem("std_done"), sem("rstd_done"), sem("ob_done"))
        waits_passed = sem("waits_passed")
        arrived = sem("arrived")
        g_idx, g_gathered, g_spread, g_hot, g_coef, g_masked, g_scaled, g_diag, g_z, g_zcopied, g_msg, g_added = (
            sem(f"g_{n}") for n in ("idx", "gathered", "spread", "hot", "coef", "masked", "scaled", "diag",
                                    "z", "zcopied", "msg", "added"))

        def load_rows(eng, nat, table, rows, done):
            if rows is None:
                eng.dma_start(nat[LAST:NR, 0:EL], table[LAST * ER:E].rearrange("(p e) -> p e", e=EL)).then_inc(done, 16)
            else:
                a, b = rows
                eng.dma_start(nat[a:b, :], table[a * ER:b * ER].rearrange("(p e) -> p e", e=ER)).then_inc(done, 16)

        PAD0 = LAST // 32 * 32

        def sync_load(sp, k, n):
            rows = N - k * P if isinstance(k, int) and k == NBLK - 1 else P
            sp.wait_ge(y_done, n)
            sp.wait_ge(xbT_done, n)
            sp.dma_start(xb[0:rows, :], x[ds(k * P, rows), :]).then_inc(x_in, 16)

        def sync_store(sp, k, n):
            rows = N - k * P if isinstance(k, int) and k == NBLK - 1 else P
            sp.wait_ge(ob_done, n + 1)
            sp.dma_start(out[ds(k * P, rows), :], ob[0:rows, :]).then_inc(stored, 16)

        def pe_xbT(pe, n):

            pe.wait_ge(x_in, n * 16 + 16)
            pe.wait_ge(xbT_copied, n)
            pe.wait_ge(h_done, n)
            carry_waits(pe)
            nc.tensor.transpose(xbT_ps, xb[:, :], ident[:, :]).then_inc(xbT_done, 1)

        def pe_fin(pe, n):
            pe.wait_ge(accb_done, n + 1)
            pe.wait_ge(xbT_copied, n + 1)
            pe.wait_ge(h_done, n)
            nc.tensor.matmul(fin_ps, accb[:, :], acc_aug[:, :], start=True, stop=False)
            nc.tensor.matmul(fin_ps, xbT[:, :], loop_aug[:, :], start=False, stop=True).then_inc(fin_done, 1)

        def act_xbT(act, n):
            act.wait_ge(xbT_done, n + 1)
            act.wait_ge(fin_done, n)
            nc.scalar.copy(xbT[0:D, :], xbT_ps).then_inc(xbT_copied, 1)

        def act_accb(act, k, n):
            act.wait_ge(fin_done, n)
            nc.scalar.copy(accb[:, :], acc[:, ds(k * P, P)]).then_inc(accb_done, 1)

        def act_relu(act, n):
            act.wait_ge(norm_done, n + 1)
            act.wait_ge(y_done, n)
            nc.scalar.activation(h[:, :], fin_ps[:, 0:D], ACT.Relu, scale=norm[:, :]).then_inc(h_done, 1)

        def act_std(act, n):
            act.wait_ge(mv_done, n + 1)
            act.wait_ge(rstd_done, n)
            nc.scalar.activation(std[:, :], mv[:, 1:2], ACT.Sqrt, bias=eps[:, :]).then_inc(std_done, 1)

        def dve_norm(dve, n):
            dve.wait_ge(fin_done, n + 1)
            dve.wait_ge(h_done, n)
            nc.vector.reciprocal(norm[:, :], fin_ps[:, D:D1]).then_inc(norm_done, 1)

        def dve_layernorm(dve, n):
            dve.wait_ge(h_done, n + 1)
            dve.wait_ge(x_in, n * 16 + 16)
            nc.vector.tensor_tensor(y[:, :], h[:, :], xb[:, :], ALU.add).then_inc(y_done, 1)
            dve.wait_ge(y_done, n + 1)
            nc.vector.bn_stats(stats[:, :], y[:, :]).then_inc(stats_done, 1)
            dve.wait_ge(stats_done, n + 1)
            carry_waits(dve)
            nc.vector.bn_aggr(mv[:, :], stats[:, :]).then_inc(mv_done, 1)

        def dve_out(dve, n):
            dve.wait_ge(std_done, n + 1)
            nc.vector.reciprocal(rstd[:, :], std[:, :]).then_inc(rstd_done, 1)
            dve.wait_ge(rstd_done, n + 1)
            dve.wait_ge(stored, n * 16)
            nc.vector.tensor_scalar(ob[:, :], y[:, :], mv[:, 0:1], rstd[:, :],
                                    ALU.subtract, ALU.mult).then_inc(ob_done, 1)

        def carry_waits(eng):
            eng.sem_inc(waits_passed, 1)

        def general_rounds():
            full = EL // P
            return [(0, LAST, 0, CR, P), (LAST, NR, 0, full, P), (LAST, NR, full, CL, EL - full * P)]

        def general(eng, nloads, body):
            for i0, i1, j0, j1, edges in general_rounds():
                with eng.Fori(i0, i1) as i:
                    with eng.Fori(j0, j1) as j:
                        body(i, j, edges)

        def rendezvous(eng, *made):
            for s in made:
                eng.sem_inc(s, 1)
            eng.drain().then_inc(arrived, 1)
            eng.wait_ge(arrived, 5)

        block = ctx.enter_context(nc.Block())

        @block.sync
        def _(sp):
            load_rows(sp, src_nat, src, (0, PAD0), src_in)
            load_rows(sp, dst_nat, dst, (0, PAD0), dst_in)
            load_rows(sp, typ_nat, etype, (0, PAD0), typ_in)
            for n, (nat, table, done) in enumerate(((src_nat, src, src_in), (dst_nat, dst, dst_in),
                                                    (typ_nat, etype, typ_in))):
                sp.wait_ge(pads_set, n + 1)
                load_rows(sp, nat, table, (PAD0, LAST), done)
                load_rows(sp, nat, table, None, done)
            sp.dma_start(wc[0:NT, 0:NB], w_comp).then_inc(wc_set, 16)
            sp.dma_start(wc[NT:P, 0:NB], w_comp).then_inc(wc_set, 16)
            sp.wait_ge(W_set, 4)
            sp.dma_start(W[0:D, 0:NB, 0:D], weight.rearrange("b i o -> i b o")).then_inc(w_in, 16)
            sp.dma_start(loop_aug[0:D, 0:D], loop_w).then_inc(w_in, 16)
            sp.dma_start(loop_aug[D:D1, 0:D], bias.rearrange("(a o) -> a o", a=1)).then_inc(w_in, 16)
            sp.wait_ge(ident_cast, 2)
            sp.dma_start(acc_aug[D:D1, 0:D], bias.rearrange("(a o) -> a o", a=1)).then_inc(w_in, 16)
            sp.wait_ge(lo_set, 1)
            sp.dma_start(base_row[0:1, :].rearrange("a (r c) -> a r c", c=CR), lo_i[:, :]).then_inc(base_in, 16)

            def finish_round(k):
                sync_load(sp, k, k)
                sync_store(sp, k, k)

            finish_round(0)
            with sp.Fori(1, NBLK - 1) as k:
                finish_round(k)
            finish_round(NBLK - 1)
            sp.wait_ge(stored, 16 * NBLK)
            sp.wait_ge(odd_out, 1)
            redo = sp.value_load(odd_i[0:1, 0:1], min_val=0, max_val=1)
            with sp.If(redo == 1):
                rendezvous(sp)
                with sp.Fori(0, NBLK - 1) as k:
                    sync_load(sp, k, k + NBLK)
                    sync_store(sp, k, k + NBLK)
                sync_load(sp, NBLK - 1, 2 * NBLK - 1)
                sync_store(sp, NBLK - 1, 2 * NBLK - 1)
                sp.wait_ge(stored, 32 * NBLK)

        @block.gpsimd
        def _(pool):
            pool.memset(ident[:, :], 0.0).then_inc(pool_const, 1)
            pool.iota(iota_p[:, :], [[0, 1]], base=0, channel_multiplier=1,
                      allow_small_or_imprecise_dtypes=True).then_inc(pool_const, 1)
            pool.iota(iota_w[:, :], [[1, WIN]], base=0, channel_multiplier=0,
                      allow_small_or_imprecise_dtypes=True).then_inc(pool_const, 1)
            pool.wait_ge(pool_const, 3)
            pool.affine_select(out=ident[:, :], in_=ident[:, :], compare_op=ALU.not_equal, fill=1.0,
                               base=0, pattern=[[-1, P]], channel_multiplier=1).then_inc(pool_const, 1)

            def gather_round(i):

                for q in range(QR):
                    n = chunks_of(i, q)
                    if not n:
                        continue
                    pool.wait_ge(idx_ready[q], i + 1)
                    pool.wait_ge(z_done[q], i)
                    carry_waits(pool)
                    for c in range(n):
                        pool.indirect_dma_start(
                            out=xg[:, q, c, 0:D], out_offset=None, in_=x[:, :],
                            in_offset=bass.IndirectOffsetOnAxis(ap=idx[:, q, c:c + 1], axis=0),
                            bounds_check=last_node, oob_is_err=False).then_inc(gathered[q], 16)

            pool.wait_ge(xg_one, 1)
            last_node = pool.to_reg(N - 1)
            gather_round(0)
            with pool.Fori(1, LAST) as i:
                gather_round(i)
            gather_round(LAST)
            pool.wait_ge(odd_out, 1)
            redo = pool.value_load(odd_i[0:1, 0:1], min_val=0, max_val=1)
            with pool.If(redo == 1):
                rendezvous(pool)

                def body(i, j, edges):
                    c = i * CR + j
                    pool.wait_ge(g_idx, c + 2)
                    pool.wait_ge(g_z, c + 1)
                    carry_waits(pool)
                    pool.indirect_dma_start(
                        out=g_x[:, 0:D], out_offset=None, in_=x[:, :],
                        in_offset=bass.IndirectOffsetOnAxis(ap=g_idx_sb[:, :], axis=0),
                        bounds_check=last_node, oob_is_err=False).then_inc(g_gathered, 16)

                general(pool, 0, body)

        @block.scalar
        def _(act):
            act.wait_ge(src_in, 48)
            QE = CQ * P
            for q in range(QR):
                nc.scalar.copy(src_f[:, q * QE:(q + 1) * QE], src_nat[:, q * QE:(q + 1) * QE]).then_inc(src_cast, 1)
                if q == 0:
                    act.wait_ge(src_tr, 1)
                    tr = z_ps[0][:, 0:CQ * NR].rearrange("p (c r) -> p r c", c=CQ)
                    nc.scalar.copy(idx[:, 0, :], tr[:, 0, :]).then_inc(idx_ready[0], 1)
            src_v = src_t[:, :].rearrange("p (r c) -> p r c", c=CR)
            for q in range(QR):
                act.wait_ge(src_tr, q + 1)
                tr = z_ps[q % 2][:, 0:CQ * NR].rearrange("p (c r) -> p r c", c=CQ)
                if q:
                    nc.scalar.copy(idx[:, q, :], tr[:, 0, :]).then_inc(idx_ready[q], 1)
                nc.scalar.copy(src_v[:, :, q * CQ:(q + 1) * CQ], tr).then_inc(src_out, 1)
            act.wait_ge(typ_in, 48)
            nc.scalar.copy(typ_b[:, :], typ_nat[:, :]).then_inc(typ_cast, 1)
            act.wait_ge(acc_zero, 1)
            half = NPAD // 2
            nc.scalar.copy(acc[:, half:NPAD], acc[:, 0:half]).then_inc(acc_zero_act, 1)

            def edge_round(i, finish):
                for q in range(QR):
                    n = chunks_of(i, q)
                    if not n:
                        continue
                    if not (isinstance(i, int) and i == LAST):
                        act.wait_ge(gathered[q], i * (16 * CQ) + 16 * CQ)
                        if isinstance(i, int) and i == 0:
                            act.wait_ge(src_out, QR)
                        nc.scalar.copy(idx[:, q, :], src_t[:, ds(i * CR + (CR + q * CQ), CQ)]).then_inc(idx_ready[q], 1)
                    act.wait_ge(z_done[q], i + 1)
                    nc.scalar.copy(
                        Z[:, :, q * CQ * WIN:(q * CQ + n) * WIN].rearrange("p b (c w) -> p b c w", w=WIN),
                        z_ps[q % 2][0:D1, 0:n * SW].rearrange("p (c b w) -> p b c w", b=B1, w=WIN),
                    ).then_inc(z_copied[q], 1)
                    if finish and q == 1:
                        act.wait_ge(added, i * CR)
                        act_accb(act, i - LATE, i - LATE)
                        act_xbT(act, i - LATE)
                    if finish and q == 2:
                        act_relu(act, i - LATE)
                if finish:
                    act_std(act, i - LATE)

            for i in range(LATE + 1):
                edge_round(i, i >= LATE)
            with act.Fori(LATE + 1, LAST) as i:
                edge_round(i, True)
            edge_round(LAST, True)
            act.wait_ge(added, NC)
            for k in range(NBLK - LATE, NBLK):
                act_accb(act, k, k)
                act_xbT(act, k)
                act_relu(act, k)
                act_std(act, k)
            act.wait_ge(odd_out, 1)
            redo = act.value_load(odd_i[0:1, 0:1], min_val=0, max_val=1)
            with act.If(redo == 1):
                rendezvous(act, g_idx, g_zcopied)

                def body(i, j, edges):
                    c = i * CR + j
                    act.wait_ge(g_z, c + 1)
                    nc.scalar.copy(g_idx_sb[:, :], src_t[:, ds(c, 1)]).then_inc(g_idx, 1)
                    act.wait_ge(g_z, c + 2)
                    for t, bank in enumerate((z_ps[0], z_ps[1], p_ps)):
                        last = nc.scalar.copy(Z[:, :, :].rearrange("p b w -> p (b w)")[:, t * 3 * P:(t + 1) * 3 * P],
                                              bank[0:D1, 0:3 * P])
                    last.then_inc(g_zcopied, 1)

                general(act, 0, body)
                act.wait_ge(g_added, E + 1)
                with act.Fori(0, NBLK) as k:
                    act_accb(act, k, k + NBLK)
                    act_xbT(act, k + NBLK)
                    act_relu(act, k + NBLK)
                    act_std(act, k + NBLK)

        @block.vector
        def _(dve):
            nsteps = [0]

            def then(ins):
                nsteps[0] += 1
                ins.then_inc(step, 1)
                dve.wait_ge(step, nsteps[0])

            nc.vector.memset(src_nat[PAD0:NR, EL:ER], 0).then_inc(pads_set, 1)
            nc.vector.memset(dst_nat[PAD0:NR, EL:ER], N - 1).then_inc(pads_set, 1)
            nc.vector.memset(typ_nat[PAD0:NR, EL:ER], NT).then_inc(pads_set, 1)
            nc.vector.memset(xg[:, :, :, D:D1], 1.0).then_inc(xg_one, 1)
            nc.vector.memset(W[:, :, :], 0.0).then_inc(W_set, 1)
            nc.vector.memset(loop_aug[:, :], 0.0).then_inc(W_set, 1)
            nc.vector.memset(ones[:, :], 1.0)
            nc.vector.memset(eps[:, :], EPS)
            dve.wait_ge(W_set, 2)
            nc.vector.memset(W[D:D1, NB:B1, D:D1], 1.0).then_inc(W_set, 1)
            nc.vector.memset(loop_aug[D:D1, D:D1], 1.0).then_inc(W_set, 1)
            nc.vector.memset(xbT[D:D1, :], 1.0)
            nc.vector.memset(g_x[:, D:D1], 1.0)
            nc.vector.memset(xb[:, :], 0.0)
            dve.wait_ge(dst_in, 48)
            dv = dst_nat[:, :].rearrange("r (c e) -> r c e", e=P)
            nc.vector.tensor_reduce(lo[:, :], dv, AX.X, ALU.min)
            then(nc.vector.tensor_reduce(hi[:, :], dv, AX.X, ALU.max))
            nc.vector.tensor_copy(lo_i[:, :], lo[:, :]).then_inc(lo_set, 1)
            then(nc.vector.tensor_tensor(span[:, :], hi[:, :], lo[:, :], ALU.subtract))
            then(nc.vector.tensor_scalar(wide[:, :], span[:, :], float(WIN), None, ALU.is_ge))
            then(nc.vector.scalar_tensor_tensor(out=shift[:, :], in0=wide[:, :], scalar=-FAR, in1=lo[:, :],
                                                op0=ALU.mult, op1=ALU.add))
            rv = rel_f[:, :].rearrange("r (c e) -> r c e", e=P)
            for q in range(QR):
                cs = slice(q * CQ, (q + 1) * CQ)
                nc.vector.tensor_tensor(rv[:, cs, :], dv[:, cs, :],
                                        shift[:, cs].unsqueeze(2).broadcast_to([NR, CQ, P]),
                                        ALU.subtract).then_inc(rel_set, 1)
            dve.wait_ge(pool_const, 4)
            nc.vector.tensor_copy(ident_b[:, :], ident[:, :]).then_inc(ident_cast, 1)
            nc.vector.tensor_copy(acc_aug[:, :], ident[0:D1, 0:D1]).then_inc(ident_cast, 1)
            then(nc.vector.tensor_scalar(type_hi[:, :], iota_p[:, :], float(NT), -float(NT), ALU.is_ge, ALU.mult))
            then(nc.vector.tensor_tensor(type_p[:, :], iota_p[:, :], type_hi[:, :], ALU.add))
            then(nc.vector.memset(wc[:, NB:B1], 1.0))
            dve.wait_ge(wc_set, 32)
            then(nc.vector.tensor_copy(wc_hi[:, :], wc[:, :]))
            then(nc.vector.tensor_tensor(wc_rest[:, :], wc[:, :], wc_hi[:, :], ALU.subtract))
            nc.vector.tensor_copy(wc_a[0:NT, :], wc_hi[0:NT, :])
            then(nc.vector.tensor_copy(wc_a[NT:P, :], wc_rest[NT:P, :]))
            then(nc.vector.tensor_copy(wc_b[:, :], wc_rest[:, :]))
            then(nc.vector.tensor_tensor(wc_low[:, :], wc_rest[:, :], wc_b[:, :], ALU.subtract))
            then(nc.vector.memset(wc_b[:, :], 0.0))
            nc.vector.tensor_copy(wc_b[0:NT, :], wc_low[0:NT, :]).then_inc(wc_split, 1)
            rel_v = rel_t[:, :].rearrange("p (r c) -> p r c", c=CR)
            for q in range(QR):
                dve.wait_ge(rel_tr, q + 1)
                last = nc.vector.tensor_copy(
                    rel_v[:, :, q * CQ:(q + 1) * CQ],
                    (z_ps[0] if q % 2 else p_ps)[:, 0:CQ * NR].rearrange("p (c r) -> p r c", c=CQ)).then_inc(rel_out, 1)

            def edge_round(i, finish):
                n_all = sum(chunks_of(i, q) for q in range(QR))
                dve.wait_ge(s_done[(n_all - 1) // CQ], i)
                if isinstance(i, int) and i == 0:
                    dve.wait_ge(rel_out, QR)
                nc.vector.tensor_tensor(
                    node_1h[:, 0:n_all, :],
                    iota_w[:, :].unsqueeze(1).broadcast_to([P, n_all, WIN]),
                    rel_t[:, ds(i * CR, n_all)].unsqueeze(2).broadcast_to([P, n_all, WIN]),
                    ALU.is_equal).then_inc(node_hot, 1)

                def hot(q):
                    n = chunks_of(i, q)
                    if not n:
                        return
                    dve.wait_ge(typ_spread[q], i + 1)
                    if q >= 2:
                        dve.wait_ge(cf_done[q - 2], i + 1)
                    else:
                        dve.wait_ge(cf_done[q + 2], i)
                    nc.vector.tensor_scalar(type_1h[:, q % 2, 0:n * P], typ_ps[q % 2][:, 0:n * P], type_p[:, :], None,
                                            ALU.is_equal).then_inc(type_hot[q], 1)

                def spread(q):
                    n = chunks_of(i, q)
                    if not n:
                        return
                    if q == 0:
                        dve.wait_ge(node_hot, i + 1)
                    dve.wait_ge(cf_done[q], i + 1)
                    dve.wait_ge(z_done[q], i)
                    nc.vector.tensor_tensor(
                        S[:, q, 0:n * SW].rearrange("p (c b w) -> p c b w", b=B1, w=WIN),
                        node_1h[:, q * CQ:q * CQ + n, :].unsqueeze(2).broadcast_to([P, n, B1, WIN]),
                        cf_slot(q)[:, 0:n, :].unsqueeze(3).broadcast_to([P, n, B1, WIN]),
                        ALU.mult).then_inc(s_done[q], 1)

                hot(0)
                hot(1)
                spread(0)
                hot(2)
                spread(1)
                if not (isinstance(i, int) and i == 0):
                    add_round(i - 1, CR)
                hot(3)
                spread(2)
                if finish:
                    dve_norm(dve, i - LATE)
                spread(3)
                if finish:
                    dve_layernorm(dve, i - LATE)
                    dve_out(dve, i - LATE)

            def add_round(r, n):
                dve.wait_ge(projected, r + 1)
                for g in range(0, n, CQ):
                    m = min(CQ, n - g)
                    _, bases = nc.values_load_multi_w_load_instructions(
                        base_row[0:1, ds(r * CR + g, m)], [mybir.EngineType.DVE], min_val=0, max_val=N - 1,
                        skip_runtime_bounds_check_because="a chunk's smallest destination is a node's number")
                    for c in range(m):
                        at = acc[:, ds(bases[c], WIN)]
                        dve.wait_ge(added, r * CR + (g + c))
                        nc.vector.tensor_tensor(at, p_ps[0:D1, (g + c) * WIN:(g + c + 1) * WIN], at,
                                                ALU.add).then_inc(added, 1)

            half = NPAD // 2
            nc.vector.memset(acc[:, 0:half], 0.0).then_inc(acc_zero, 1)
            edge_round(0, False)
            dve.wait_ge(base_in, 16)
            then(nc.vector.tensor_reduce(round_lo[:, :], lo[:, :], AX.X, ALU.min))
            then(nc.vector.tensor_scalar(finished_to[:, :], iota_p[:, :], float(P), -float((LATE - 1) * P), ALU.mult, ALU.add))
            nc.vector.tensor_tensor(odd[:, 0:1], round_lo[:, :], finished_to[0:NR, :], ALU.is_lt)
            nc.vector.tensor_reduce(odd[:, 1:2], wide[:, :], AX.X, ALU.max).then_inc(odd_set, 1)
            dve.wait_ge(odd_sum, 1)
            nc.vector.tensor_scalar(odd_i[:, :], typ_ps[0][0:1, 0:1], 0.0, None, ALU.is_gt).then_inc(odd_out, 1)
            dve.wait_ge(acc_zero_act, 1)
            for i in range(1, LATE + 1):
                edge_round(i, i >= LATE)
            with dve.Fori(LATE + 1, LAST) as i:
                edge_round(i, True)
            edge_round(LAST, True)
            add_round(LAST, CL)
            for k in range(NBLK - LATE, NBLK):
                dve_norm(dve, k)
                dve_layernorm(dve, k)
                dve_out(dve, k)
            redo = dve.value_load(odd_i[0:1, 0:1], min_val=0, max_val=1)
            with dve.If(redo == 1):
                rendezvous(dve, g_hot, g_masked, g_scaled, g_diag, g_added)
                diag = S[:, :, :].rearrange("p q s -> p (q s)")[:, 0:B1 * P].rearrange("p (b e) -> p b e", e=P)

                def body(i, j, edges):
                    c = i * CR + j
                    dve.wait_ge(g_spread, c + 2)
                    nc.vector.tensor_scalar(type_1h[:, 0, 0:P], typ_ps[0][:, 0:P], type_p[:, :], None,
                                            ALU.is_equal).then_inc(g_hot, 1)
                    nc.vector.tensor_scalar(g_mask[:, :], rel_t[:, ds(c, 1)], FAR, None, ALU.is_ge).then_inc(g_masked, 1)
                    dve.wait_ge(g_masked, c + 2)
                    dve.wait_ge(g_coef, c + 2)
                    nc.vector.tensor_scalar(g_cf[:, :], cf_ps[0][:, 0:B1], g_mask[:, :], None,
                                            ALU.mult).then_inc(g_scaled, 1)
                    dve.wait_ge(g_scaled, c + 2)
                    nc.vector.tensor_tensor(diag, ident[:, :].unsqueeze(1).broadcast_to([P, B1, P]),
                                            g_cf[:, :].unsqueeze(2).broadcast_to([P, B1, P]),
                                            ALU.mult).then_inc(g_diag, 1)
                    dve.wait_ge(g_msg, c + 2)
                    carry_waits(dve)
                    with dve.Fori(0, edges) as e:
                        _, (node,) = nc.values_load_multi_w_load_instructions(
                            dst[ds(c * P + e, 1)].unsqueeze(0), [mybir.EngineType.DVE], min_val=0, max_val=N - 1,
                            skip_runtime_bounds_check_because="a destination is a node's number")
                        at = acc[:, ds(node, 1)]
                        dve.wait_ge(g_added, c * P + e + 1)
                        nc.vector.tensor_tensor(at, f_ps[0:D1, ds(e, 1)], at, ALU.add).then_inc(g_added, 1)

                general(dve, 0, body)
                with dve.Fori(0, NBLK) as k:
                    dve_norm(dve, k + NBLK)
                    dve_layernorm(dve, k + NBLK)
                    dve_out(dve, k + NBLK)

        @block.tensor
        def _(pe):
            pe.wait_ge(pool_const, 4)
            for q in range(QR):
                pe.wait_ge(src_cast, q + 1)
                if q >= 2:
                    pe.wait_ge(src_out, q - 1)
                for c in range(CQ):
                    j = q * CQ + c
                    last = nc.tensor.transpose(z_ps[q % 2][:, c * NR:(c + 1) * NR], src_f[:, j * P:(j + 1) * P],
                                               ident[0:NR, 0:NR])
                last.then_inc(src_tr, 1)
            for q in range(QR):
                pe.wait_ge(rel_set, q + 1)
                if q == 1:
                    pe.wait_ge(src_out, QR)
                if q >= 2:
                    pe.wait_ge(rel_out, q - 1)
                for c in range(CQ):
                    j = q * CQ + c
                    last = nc.tensor.transpose((z_ps[0] if q % 2 else p_ps)[:, c * NR:(c + 1) * NR],
                                               rel_f[:, j * P:(j + 1) * P], ident[0:NR, 0:NR])
                last.then_inc(rel_tr, 1)
            pe.wait_ge(typ_cast, 1)
            pe.wait_ge(ident_cast, 2)
            pe.wait_ge(wc_split, 1)
            pe.wait_ge(rel_out, QR)
            pe.wait_ge(w_in, 64)

            def edge_round(i, finish):
                row = ident_b[0:NR, ds(i, 1)].to_broadcast([NR, P])

                def types(q):
                    n = chunks_of(i, q)
                    if not n:
                        return
                    if q >= 2:
                        pe.wait_ge(type_hot[q - 2], i + 1)
                    else:
                        pe.wait_ge(type_hot[q + 2], i)
                    nc.tensor.matmul(typ_ps[q % 2][:, 0:n * P], row, typ_b[:, q * CQ * P:(q * CQ + n) * P],
                                     start=True, stop=True).then_inc(typ_spread[q], 1)

                def coefs(q):
                    n = chunks_of(i, q)
                    if not n:
                        return
                    pe.wait_ge(type_hot[q], i + 1)
                    pe.wait_ge(s_done[q], i)
                    for c in range(n):
                        hot = type_1h[:, q % 2, c * P:(c + 1) * P]
                        nc.tensor.matmul(cf_slot(q)[:, c, :], hot, wc_a[:, :], start=True, stop=False)
                        last = nc.tensor.matmul(cf_slot(q)[:, c, :], hot, wc_b[:, :], start=False, stop=True)
                    last.then_inc(cf_done[q], 1)

                def sums(q):
                    n = chunks_of(i, q)
                    if not n:
                        return
                    pe.wait_ge(s_done[q], i + 1)
                    pe.wait_ge(gathered[q], i * (16 * CQ) + 16 * n)
                    if q >= 2:
                        pe.wait_ge(z_copied[q - 2], i + 1)
                    else:
                        pe.wait_ge(z_copied[q + 2], i)
                    for c in range(n):
                        last = nc.tensor.matmul(z_ps[q % 2][0:D1, c * SW:(c + 1) * SW], xg[:, q, c, :],
                                                S[:, q, c * SW:(c + 1) * SW], start=True, stop=True)
                    last.then_inc(z_done[q], 1)

                types(0)
                types(1)
                coefs(0)
                types(2)
                coefs(1)
                if not (isinstance(i, int) and i == 0):
                    project(i - 1, CR)
                sums(0)
                types(3)
                coefs(2)
                sums(1)
                if finish:
                    pe_xbT(pe, i - LATE)
                coefs(3)
                sums(2)
                if finish:
                    pe_fin(pe, i - LATE)
                sums(3)

            def project(r, n):
                for q in range(-(-n // CQ)):
                    pe.wait_ge(z_copied[q], r + 1)
                pe.wait_ge(added, r * CR)
                for b in range(B1):
                    last = nc.tensor.matmul(p_ps[0:D1, 0:n * WIN], W[:, b, :], Z[:, b, 0:n * WIN],
                                            start=(b == 0), stop=(b == B1 - 1))
                last.then_inc(projected, 1)

            edge_round(0, False)
            pe.wait_ge(odd_set, 1)
            pe.wait_ge(type_hot[2], 1)
            nc.tensor.matmul(typ_ps[0][0:1, 0:1], odd[:, 0:1], ones[0:NR, :], start=True, stop=False)
            nc.tensor.matmul(typ_ps[0][0:1, 0:1], odd[:, 1:2], ones[0:NR, :], start=False, stop=True).then_inc(odd_sum, 1)
            pe.wait_ge(odd_out, 1)
            for i in range(1, LATE + 1):
                edge_round(i, i >= LATE)
            with pe.Fori(LATE + 1, LAST) as i:
                edge_round(i, True)
            edge_round(LAST, True)
            project(LAST, CL)
            for k in range(NBLK - LATE, NBLK):
                pe_xbT(pe, k)
                pe_fin(pe, k)
            redo = pe.value_load(odd_i[0:1, 0:1], min_val=0, max_val=1)
            with pe.If(redo == 1):
                rendezvous(pe, g_spread, g_coef, g_z, g_msg)
                diag = S[:, :, :].rearrange("p q s -> p (q s)")
                zv = Z[:, :, :].rearrange("p b w -> p (b w)")

                def body(i, j, edges):
                    c = i * CR + j
                    pe.wait_ge(g_hot, c + 1)
                    nc.tensor.matmul(typ_ps[0][:, 0:P], ident_b[0:NR, ds(i, 1)].to_broadcast([NR, P]),
                                     typ_b[:, ds(j * P, P)], start=True, stop=True).then_inc(g_spread, 1)
                    pe.wait_ge(g_hot, c + 2)
                    pe.wait_ge(g_scaled, c + 1)
                    nc.tensor.matmul(cf_ps[0][:, 0:B1], type_1h[:, 0, 0:P], wc_a[:, :], start=True, stop=False)
                    nc.tensor.matmul(cf_ps[0][:, 0:B1], type_1h[:, 0, 0:P], wc_b[:, :], start=False,
                                     stop=True).then_inc(g_coef, 1)
                    pe.wait_ge(g_diag, c + 2)
                    pe.wait_ge(g_gathered, c * 16 + 16)
                    pe.wait_ge(g_zcopied, c + 1)
                    for t, bank in enumerate((z_ps[0], z_ps[1], p_ps)):
                        last = nc.tensor.matmul(bank[0:D1, 0:3 * P], g_x[:, :], diag[:, t * 3 * P:(t + 1) * 3 * P],
                                                start=True, stop=True)
                    last.then_inc(g_z, 1)
                    pe.wait_ge(g_zcopied, c + 2)
                    pe.wait_ge(g_added, c * P + 1)
                    for b in range(B1):
                        last = nc.tensor.matmul(f_ps[0:D1, 0:P], W[:, b, :], zv[:, b * P:(b + 1) * P],
                                                start=(b == 0), stop=(b == B1 - 1))
                    last.then_inc(g_msg, 1)

                general(pe, 0, body)
                pe.wait_ge(g_added, E + 1)
                with pe.Fori(0, NBLK) as k:
                    pe_xbT(pe, k + NBLK)
                    pe_fin(pe, k + NBLK)


_INS = ["x", "src", "dst", "edge_type_64", "L0_gnn_weight", "L0_gnn_w_comp", "L0_gnn_loop_weight", "L0_gnn_bias"]


def kernel(**inputs):
    import numpy as np
    import concourse.bacc as bacc
    from concourse.bass_utils import run_bass_kernel_spmd as run

    nc = bacc.Bacc("TRN2", target_bir_lowering=False, num_devices=1)
    arrays, args = {}, []
    for name in _INS:
        a = np.ascontiguousarray(inputs[name])
        arrays[f"in_{name}"] = a
        args.append(nc.dram_tensor(f"in_{name}", a.shape, mybir.dt.from_np(a.dtype), kind="ExternalInput").ap())
    args.append(nc.dram_tensor("out_0", inputs["x"].shape, mybir.dt.float32, kind="ExternalOutput").ap())
    rgcn_kernel(nc, *args)
    return run(nc, [arrays], core_ids=[0]).results[0]["out_0"]
```

```python
import concourse.bass as bass
from concourse import mybir
from contextlib import ExitStack


def rgcn_kernel(nc, x, src, dst, etype, weight, w_comp, loop_w, bias, out):
    fp32, bf16, i32 = mybir.dt.float32, mybir.dt.bfloat16, mybir.dt.int32
    ALU, ACT, AX = mybir.AluOpType, mybir.ActivationFunctionType, mybir.AxisListType
    ds = bass.ds

    N, D = x.shape
    E = src.shape[0]
    NB = weight.shape[0]
    NT = w_comp.shape[0]
    P = 128
    D1 = D + 1
    NH = NB // 2
    WIN = 13
    CQ = 4
    QR = 4
    CR = CQ * QR
    ER = P * CR
    NR = -(-E // ER)
    NC = -(-E // P)
    LAST = NR - 1
    EL = E - LAST * ER
    CL = NC - LAST * CR
    NBLK = -(-N // P)
    NPAD = NBLK * P
    HW = NH * WIN
    SW = NB * WIN
    RW = CR * WIN
    FAR = 4096.0
    EPS = 1e-5
    ACC_DVE = NPAD // 4
    LATE = 2
    assert NR == NBLK and RW <= 512 and CQ * SW <= 512 and NPAD >= N + WIN
    assert 2 * NT == P and 2 * D == P and NH * P <= 512

    def chunks_of(i, q):
        if isinstance(i, int) and i == LAST:
            return max(0, min(CQ, CL - CQ * q))
        return CQ

    def ahead(i, q, by):
        return i + (q + by) // QR, (q + by) % QR

    def exists(i, q):
        return not isinstance(i, int) or (0 <= i <= LAST and chunks_of(i, q) > 0)

    ctx = ExitStack()
    with ctx:
        def sb(name, shape, dt):
            return ctx.enter_context(nc.sbuf_tensor(name, shape, dt))

        def pb(name, shape, dt=fp32):
            return ctx.enter_context(nc.psum_tensor(name, shape, dt))

        def sem(name):
            return ctx.enter_context(nc.semaphore(name))

        def sems(name, n=QR):
            return [sem(f"{name}{j}") for j in range(n)]

        src_nat = sb("src_nat", [NR, ER], i32)
        dst_nat = sb("dst_nat", [NR, ER], i32)
        typ_nat = sb("typ_nat", [NR, ER], i32)
        src_f = sb("src_f", [NR, ER], fp32)
        src0_nat = sb("src0_nat", [CR, P], i32)
        src0_f = sb("src0_f", [CR, P], fp32)
        zero = sb("zero", [D1, 1], fp32)
        rel_f = sb("rel_f", [NR, ER], fp32)
        typ_b = sb("typ_b", [NR, ER], bf16)
        src_t = sb("src_t", [P, NR * CR], fp32)
        rel_t = sb("rel_t", [P, NR * CR], fp32)
        lo = sb("lo", [NR, CR], fp32)
        hi = sb("hi", [NR, CR], fp32)
        span = sb("span", [NR, CR], fp32)
        wide = sb("wide", [NR, CR], fp32)
        shift = sb("shift", [NR, CR], fp32)
        lo_i = sb("lo_i", [NR, CR], i32)
        base_row = sb("base_row", [1, NR * CR], i32)
        round_lo = sb("round_lo", [NR, 1], fp32)
        finished_to = sb("finished_to", [P, 1], fp32)
        odd = sb("odd", [NR, 2], fp32)
        odd_i = sb("odd_i", [1, 1], i32)
        iota_p = sb("iota_p", [P, 1], fp32)
        type_p = sb("type_p", [P, 1], fp32)
        type_hi = sb("type_hi", [P, 1], fp32)
        iota_w = sb("iota_w", [P, WIN], fp32)
        ident = sb("ident", [P, P], fp32)
        ident_b = sb("ident_b", [P, P], bf16)
        ones = sb("ones", [P, 1], fp32)
        eps = sb("eps", [P, 1], fp32)
        wc = sb("wc", [P, NB], fp32)
        wc_rest = sb("wc_rest", [P, NB], fp32)
        wc_low = sb("wc_low", [P, NB], fp32)
        wc_hi = sb("wc_hi", [P, NB], bf16)
        wc_a = sb("wc_a", [P, NB], bf16)
        wc_b = sb("wc_b", [P, NB], bf16)
        W = sb("W", [P, NH, D1], fp32)
        count_w = sb("count_w", [P, D1], bf16)
        loop_aug = sb("loop_aug", [D1, D1], fp32)
        acc_aug = sb("acc_aug", [D1, D1], fp32)
        idx = sb("idx", [P, QR, CQ], i32)
        xg = sb("xg", [P, QR, CQ, D], fp32)
        type_1h = sb("type_1h", [P, 2, CQ * P], bf16)
        node_1h = sb("node_1h", [P, NR * RW], bf16)
        S = sb("S", [P, QR, CQ * SW], fp32)
        Z = sb("Z", [P, NH, RW], fp32)
        acc = sb("acc", [D1, NPAD], fp32)
        xb = sb("xb", [P, D], fp32)
        xbT = sb("xbT", [D1, P], fp32)
        accb = sb("accb", [D1, P], fp32)
        norm = sb("norm", [P, 1], fp32)
        deg1 = sb("deg1", [P, 1], fp32)
        h = sb("h", [P, D], fp32)
        y = sb("y", [P, D], fp32)
        stats = sb("stats", [P, 6], fp32)
        mv = sb("mv", [P, 2], fp32)
        std = sb("std", [P, 1], fp32)
        rstd = sb("rstd", [P, 1], fp32)
        ob = sb("ob", [P, D], fp32)
        g_idx_sb = sb("g_idx_sb", [P, 1], i32)
        g_x = sb("g_x", [P, D], fp32)
        g_mask = sb("g_mask", [P, 1], fp32)
        g_cf = sb("g_cf", [P, NB], fp32)
        g_count = sb("g_count", [P, P], bf16)

        typ_ps = [pb(f"typ_ps{k}", [P, 512]) for k in range(2)]
        cf_ps = [pb(f"cf_ps{k}", [P, 512]) for k in range(2)]
        z_ps = [pb(f"z_ps{k}", [P, 512]) for k in range(2)]
        p_ps = pb("p_ps", [P, 512])
        f_ps = pb("f_ps", [P, 512])
        xbT_ps = f_ps[0:D, 0:P]
        rel_banks = [p_ps, f_ps, cf_ps[0], cf_ps[1]]
        fin_ps = f_ps[:, 256:256 + D1]

        def cf_slot(q):
            return cf_ps[q % 2][:, (q // 2) * 64:(q // 2) * 64 + CQ * NB].rearrange("p (c b) -> p c b", b=NB)

        src_in, dst_in, typ_in, w_in = sem("src_in"), sem("dst_in"), sem("typ_in"), sem("w_in")
        pads_set, wc_set, W_set = sem("pads_set"), sem("wc_set"), sem("W_set")
        base_in = sem("base_in")
        pool_const, dve_const = sem("pool_const"), sem("dve_const")
        src0_in, src0_cast, src0_tr = sem("src0_in"), sem("src0_cast"), sem("src0_tr")
        src_cast, src_tr, src_out = sem("src_cast"), sem("src_tr"), sem("src_out")
        rel_set, rel_tr, rel_out = sem("rel_set"), sem("rel_tr"), sem("rel_out")
        typ_cast, lo_set, odd_set, odd_sum, odd_out = (
            sem("typ_cast"), sem("lo_set"), sem("odd_set"), sem("odd_sum"), sem("odd_out"))
        ident_cast, wc_split = sem("ident_cast"), sem("wc_split")
        step = sem("step")
        acc_zero_act, zero_set, count_set = sem("acc_zero_act"), sem("zero_set"), sem("count_set")
        idx_ready, gathered = sems("idx_ready"), sems("gathered")
        typ_spread, type_hot = sems("typ_spread"), sems("type_hot")
        cf_done, s_done, z_done, z_copied = sems("cf_done"), sems("s_done"), sems("z_done"), sems("z_copied")
        node_hot, projected, added = sem("node_hot"), sem("projected"), sem("added")
        x_in, stored = sem("x_in"), sem("stored")
        xbT_done, xbT_copied, accb_done, fin_done = sem("xbT_done"), sem("xbT_copied"), sem("accb_done"), sem("fin_done")
        deg1_done, norm_done, h_done, y_done = sem("deg1_done"), sem("norm_done"), sem("h_done"), sem("y_done")
        stats_done, mv_done, std_done, rstd_done, ob_done = (
            sem("stats_done"), sem("mv_done"), sem("std_done"), sem("rstd_done"), sem("ob_done"))
        waits_passed = sem("waits_passed")
        arrived = sem("arrived")
        g_idx, g_gathered, g_spread, g_hot, g_coef, g_masked, g_scaled, g_diag, g_z, g_zcopied, g_msg, g_added = (
            sem(f"g_{n}") for n in ("idx", "gathered", "spread", "hot", "coef", "masked", "scaled", "diag",
                                    "z", "zcopied", "msg", "added"))

        def load_rows(eng, nat, table, rows, done):
            if rows is None:
                eng.dma_start(nat[LAST:NR, 0:EL], table[LAST * ER:E].rearrange("(p e) -> p e", e=EL)).then_inc(done, 16)
            else:
                a, b = rows
                eng.dma_start(nat[a:b, :], table[a * ER:b * ER].rearrange("(p e) -> p e", e=ER)).then_inc(done, 16)

        PAD0 = LAST // 32 * 32

        def sync_load(sp, k, n):
            rows = N - k * P if isinstance(k, int) and k == NBLK - 1 else P
            sp.wait_ge(y_done, n)
            sp.wait_ge(xbT_done, n)
            sp.dma_start(xb[0:rows, :], x[ds(k * P, rows), :]).then_inc(x_in, 16)

        def sync_store(sp, k, n):
            rows = N - k * P if isinstance(k, int) and k == NBLK - 1 else P
            sp.wait_ge(ob_done, n + 1)
            sp.dma_start(out[ds(k * P, rows), :], ob[0:rows, :]).then_inc(stored, 16)

        def pe_xbT(pe, n):

            pe.wait_ge(x_in, n * 16 + 16)
            pe.wait_ge(xbT_copied, n)
            pe.wait_ge(h_done, n)
            carry_waits(pe)
            nc.tensor.transpose(xbT_ps, xb[:, :], ident[:, :]).then_inc(xbT_done, 1)

        def pe_fin(pe, n):
            pe.wait_ge(accb_done, n + 1)
            pe.wait_ge(xbT_copied, n + 1)
            pe.wait_ge(h_done, n)
            nc.tensor.matmul(fin_ps, accb[:, :], acc_aug[:, :], start=True, stop=False)
            nc.tensor.matmul(fin_ps, xbT[:, :], loop_aug[:, :], start=False, stop=True).then_inc(fin_done, 1)

        def act_xbT(act, n):
            act.wait_ge(xbT_done, n + 1)
            act.wait_ge(fin_done, n)
            nc.scalar.copy(xbT[0:D, :], xbT_ps).then_inc(xbT_copied, 1)

        def act_accb(act, k, n):
            act.wait_ge(fin_done, n)
            nc.scalar.copy(accb[:, :], acc[:, ds(k * P, P)]).then_inc(accb_done, 1)

        def act_relu(act, n):
            act.wait_ge(norm_done, n + 1)
            act.wait_ge(y_done, n)
            nc.scalar.activation(h[:, :], fin_ps[:, 0:D], ACT.Relu, scale=norm[:, :]).then_inc(h_done, 1)

        def act_std(act, n):
            act.wait_ge(mv_done, n + 1)
            act.wait_ge(rstd_done, n)
            nc.scalar.activation(std[:, :], mv[:, 1:2], ACT.Sqrt, bias=eps[:, :]).then_inc(std_done, 1)

        def dve_norm(dve, n):
            dve.wait_ge(fin_done, n + 1)
            dve.wait_ge(h_done, n)
            nc.vector.reciprocal(norm[:, :], fin_ps[:, D:D1]).then_inc(norm_done, 1)

        def dve_layernorm(dve, n):
            dve.wait_ge(h_done, n + 1)
            dve.wait_ge(x_in, n * 16 + 16)
            nc.vector.tensor_tensor(y[:, :], h[:, :], xb[:, :], ALU.add).then_inc(y_done, 1)
            dve.wait_ge(y_done, n + 1)
            nc.vector.bn_stats(stats[:, :], y[:, :]).then_inc(stats_done, 1)
            dve.wait_ge(stats_done, n + 1)
            carry_waits(dve)
            nc.vector.bn_aggr(mv[:, :], stats[:, :]).then_inc(mv_done, 1)

        def dve_out(dve, n):
            dve.wait_ge(std_done, n + 1)
            nc.vector.reciprocal(rstd[:, :], std[:, :]).then_inc(rstd_done, 1)
            dve.wait_ge(rstd_done, n + 1)
            dve.wait_ge(stored, n * 16)
            nc.vector.tensor_scalar(ob[:, :], y[:, :], mv[:, 0:1], rstd[:, :],
                                    ALU.subtract, ALU.mult).then_inc(ob_done, 1)

        def carry_waits(eng):
            eng.sem_inc(waits_passed, 1)

        def general_rounds():
            full = EL // P
            return [(0, LAST, 0, CR, P), (LAST, NR, 0, full, P), (LAST, NR, full, CL, EL - full * P)]

        def general(eng, nloads, body):
            for i0, i1, j0, j1, edges in general_rounds():
                with eng.Fori(i0, i1) as i:
                    with eng.Fori(j0, j1) as j:
                        body(i, j, edges)

        def rendezvous(eng, *made):
            for s in made:
                eng.sem_inc(s, 1)
            eng.drain().then_inc(arrived, 1)
            eng.wait_ge(arrived, 5)

        block = ctx.enter_context(nc.Block())

        @block.sync
        def _(sp):
            sp.dma_start(src0_nat[:, :], src[0:ER].rearrange("(c e) -> c e", e=P)).then_inc(src0_in, 16)
            load_rows(sp, dst_nat, dst, (0, PAD0), dst_in)
            sp.dma_start(wc[0:NT, 0:NB], w_comp).then_inc(wc_set, 16)
            sp.dma_start(wc[NT:P, 0:NB], w_comp).then_inc(wc_set, 16)
            for n, (nat, table, done) in enumerate(((dst_nat, dst, dst_in), (typ_nat, etype, typ_in),
                                                    (src_nat, src, src_in))):
                if n:
                    load_rows(sp, nat, table, (0, PAD0), done)
                sp.wait_ge(pads_set, n + 1)
                load_rows(sp, nat, table, (PAD0, LAST), done)
                load_rows(sp, nat, table, None, done)
            sp.wait_ge(W_set, 3)
            sp.wait_ge(count_set, 4)
            sp.dma_start(W[0:D, :, 0:D], weight[0:NH].rearrange("b i o -> i b o")).then_inc(w_in, 16)
            sp.dma_start(W[D:P, :, 0:D], weight[NH:NB].rearrange("b i o -> i b o")).then_inc(w_in, 16)
            sp.dma_start(loop_aug[0:D, 0:D], loop_w).then_inc(w_in, 16)
            sp.dma_start(loop_aug[D:D1, 0:D], bias.rearrange("(a o) -> a o", a=1)).then_inc(w_in, 16)
            sp.wait_ge(ident_cast, 2)
            sp.dma_start(acc_aug[D:D1, 0:D], bias.rearrange("(a o) -> a o", a=1)).then_inc(w_in, 16)
            sp.wait_ge(lo_set, 1)
            sp.dma_start(base_row[0:1, :].rearrange("a (r c) -> a r c", c=CR), lo_i[:, :]).then_inc(base_in, 16)

            def finish_round(k):
                sync_load(sp, k, k)
                sync_store(sp, k, k)

            finish_round(0)
            with sp.Fori(1, NBLK - 1) as k:
                finish_round(k)
            finish_round(NBLK - 1)
            sp.wait_ge(stored, 16 * NBLK)
            sp.wait_ge(odd_out, 1)
            redo = sp.value_load(odd_i[0:1, 0:1], min_val=0, max_val=1)
            with sp.If(redo == 1):
                rendezvous(sp)
                with sp.Fori(0, NBLK - 1) as k:
                    sync_load(sp, k, k + NBLK)
                    sync_store(sp, k, k + NBLK)
                sync_load(sp, NBLK - 1, 2 * NBLK - 1)
                sync_store(sp, NBLK - 1, 2 * NBLK - 1)
                sp.wait_ge(stored, 32 * NBLK)

        @block.gpsimd
        def _(pool):
            pool.memset(ident[:, :], 0.0).then_inc(pool_const, 1)
            pool.iota(iota_p[:, :], [[0, 1]], base=0, channel_multiplier=1,
                      allow_small_or_imprecise_dtypes=True).then_inc(pool_const, 1)
            pool.iota(iota_w[:, :], [[1, WIN]], base=0, channel_multiplier=0,
                      allow_small_or_imprecise_dtypes=True).then_inc(pool_const, 1)
            pool.wait_ge(pool_const, 3)
            pool.affine_select(out=ident[:, :], in_=ident[:, :], compare_op=ALU.not_equal, fill=1.0,
                               base=0, pattern=[[-1, P]], channel_multiplier=1).then_inc(pool_const, 1)

            def gather_round(i):

                for q in range(QR):
                    n = chunks_of(i, q)
                    if not n:
                        continue
                    pool.wait_ge(idx_ready[q], i + 1)
                    pool.wait_ge(z_done[q], i)
                    carry_waits(pool)
                    for c in range(n):
                        pool.indirect_dma_start(
                            out=xg[:, q, c, 0:D], out_offset=None, in_=x[:, :],
                            in_offset=bass.IndirectOffsetOnAxis(ap=idx[:, q, c:c + 1], axis=0),
                            bounds_check=last_node, oob_is_err=False).then_inc(gathered[q], 16)


            pool.memset(W[:, :, :], 0.0).then_inc(W_set, 1)
            pool.memset(loop_aug[:, :], 0.0).then_inc(W_set, 1)
            pool.memset(count_w[:, 0:D], 0.0).then_inc(count_set, 1)
            pool.memset(count_w[:, D:D1], 1.0).then_inc(count_set, 1)
            pool.memset(xb[:, :], 0.0).then_inc(count_set, 1)
            last_node = pool.to_reg(N - 1)
            gather_round(0)
            with pool.Fori(1, LAST) as i:
                gather_round(i)
            gather_round(LAST)
            pool.wait_ge(odd_out, 1)
            redo = pool.value_load(odd_i[0:1, 0:1], min_val=0, max_val=1)
            with pool.If(redo == 1):
                rendezvous(pool)

                def body(i, j, edges):
                    c = i * CR + j
                    pool.wait_ge(g_idx, c + 2)
                    pool.wait_ge(g_z, c + 1)
                    carry_waits(pool)
                    pool.indirect_dma_start(
                        out=g_x[:, 0:D], out_offset=None, in_=x[:, :],
                        in_offset=bass.IndirectOffsetOnAxis(ap=g_idx_sb[:, :], axis=0),
                        bounds_check=last_node, oob_is_err=False).then_inc(g_gathered, 16)

                general(pool, 0, body)

        @block.scalar
        def _(act):
            act.wait_ge(zero_set, 1)
            nc.scalar.copy(acc[:, ACC_DVE:NPAD],
                           zero[:, :].to_broadcast([D1, NPAD - ACC_DVE])).then_inc(acc_zero_act, 1)
            act.wait_ge(typ_in, 48)
            nc.scalar.copy(typ_b[:, :], typ_nat[:, :]).then_inc(typ_cast, 1)
            act.wait_ge(src_in, 48)
            QE = CQ * P
            for q in range(QR):
                nc.scalar.copy(src_f[:, q * QE:(q + 1) * QE], src_nat[:, q * QE:(q + 1) * QE]).then_inc(src_cast, 1)
            src_v = src_t[:, :].rearrange("p (r c) -> p r c", c=CR)
            for q in range(QR):
                act.wait_ge(src_tr, q + 1)
                tr = z_ps[q % 2][:, 0:CQ * NR].rearrange("p (c r) -> p r c", c=CQ)

                nc.scalar.copy(src_v[:, :, q * CQ:(q + 1) * CQ], tr).then_inc(src_out, 1)


            def edge_round(i, finish):
                for q in range(QR):
                    n = chunks_of(i, q)
                    if not n:
                        continue
                    if finish and q == 2:
                        act.wait_ge(added, i * CR)
                        act_accb(act, i - LATE, i - LATE)
                        act_xbT(act, i - LATE)
                    if not (isinstance(i, int) and i == LAST):
                        act.wait_ge(gathered[q], i * (16 * CQ) + 16 * CQ)
                        if isinstance(i, int) and i == 0:
                            act.wait_ge(src_out, QR)
                        nc.scalar.copy(idx[:, q, :], src_t[:, ds(i * CR + (CR + q * CQ), CQ)]).then_inc(idx_ready[q], 1)
                    act.wait_ge(z_done[q], i + 1)
                    nc.scalar.copy(
                        Z[:, :, q * CQ * WIN:(q * CQ + n) * WIN].rearrange("p b (c w) -> p b c w", w=WIN),
                        z_ps[q % 2][:, 0:n * HW].rearrange("p (c b w) -> p b c w", b=NH, w=WIN),
                    ).then_inc(z_copied[q], 1)
                if finish:
                    act_relu(act, i - LATE)
                    act_std(act, i - LATE)

            for i in range(LATE + 1):
                edge_round(i, i >= LATE)
            with act.Fori(LATE + 1, LAST) as i:
                edge_round(i, True)
            edge_round(LAST, True)
            act.wait_ge(added, NC)
            for k in range(NBLK - LATE, NBLK):
                act_accb(act, k, k)
                act_xbT(act, k)
                act_relu(act, k)
                act_std(act, k)
            act.wait_ge(odd_out, 1)
            redo = act.value_load(odd_i[0:1, 0:1], min_val=0, max_val=1)
            with act.If(redo == 1):
                rendezvous(act, g_idx, g_zcopied)

                def body(i, j, edges):
                    c = i * CR + j
                    act.wait_ge(g_z, c + 1)
                    nc.scalar.copy(g_idx_sb[:, :], src_t[:, ds(c, 1)]).then_inc(g_idx, 1)
                    act.wait_ge(g_z, c + 2)
                    nc.scalar.copy(Z[:, :, :].rearrange("p b w -> p (b w)")[:, 0:NH * P],
                                   z_ps[0][:, 0:NH * P]).then_inc(g_zcopied, 1)

                general(act, 0, body)
                act.wait_ge(g_added, E + 1)
                with act.Fori(0, NBLK) as k:
                    act_accb(act, k, k + NBLK)
                    act_xbT(act, k + NBLK)
                    act_relu(act, k + NBLK)
                    act_std(act, k + NBLK)

        @block.vector
        def _(dve):
            nsteps = [0]

            def then(ins):
                nsteps[0] += 1
                ins.then_inc(step, 1)
                dve.wait_ge(step, nsteps[0])

            nc.vector.memset(zero[:, :], 0.0).then_inc(zero_set, 1)
            nc.vector.memset(dst_nat[PAD0:NR, EL:ER], N - 1).then_inc(pads_set, 1)
            nc.vector.memset(typ_nat[PAD0:NR, EL:ER], NT).then_inc(pads_set, 1)
            dve.wait_ge(src0_in, 16)
            nc.vector.tensor_copy(src0_f[:, :], src0_nat[:, :]).then_inc(src0_cast, 1)
            nc.vector.memset(src_nat[PAD0:NR, EL:ER], 0).then_inc(pads_set, 1)
            nc.vector.memset(xbT[D:D1, :], 1.0).then_inc(count_set, 1)
            dve.wait_ge(src0_tr, 1)
            for q in range(QR):
                nc.vector.tensor_copy(idx[:, q, :], z_ps[0][:, q * CQ:(q + 1) * CQ]).then_inc(idx_ready[q], 1)
            nc.vector.memset(eps[:, :], EPS)
            nc.vector.memset(ones[:, :], 1.0)
            dve.wait_ge(W_set, 2)
            nc.vector.memset(loop_aug[D:D1, D:D1], 1.0).then_inc(W_set, 1)
            dve.wait_ge(pool_const, 4)
            nc.vector.tensor_copy(ident_b[:, :], ident[:, :]).then_inc(ident_cast, 1)
            nc.vector.tensor_copy(acc_aug[:, :], ident[0:D1, 0:D1]).then_inc(ident_cast, 1)
            then(nc.vector.tensor_scalar(type_hi[:, :], iota_p[:, :], float(NT), -float(NT), ALU.is_ge, ALU.mult))
            then(nc.vector.tensor_tensor(type_p[:, :], iota_p[:, :], type_hi[:, :], ALU.add))

            dve.wait_ge(wc_set, 32)
            then(nc.vector.tensor_copy(wc_hi[:, :], wc[:, :]))
            then(nc.vector.tensor_tensor(wc_rest[:, :], wc[:, :], wc_hi[:, :], ALU.subtract))
            nc.vector.tensor_copy(wc_a[0:NT, :], wc_hi[0:NT, :])
            then(nc.vector.tensor_copy(wc_a[NT:P, :], wc_rest[NT:P, :]))
            then(nc.vector.tensor_copy(wc_b[:, :], wc_rest[:, :]))
            then(nc.vector.tensor_tensor(wc_low[:, :], wc_rest[:, :], wc_b[:, :], ALU.subtract))
            then(nc.vector.memset(wc_b[:, :], 0.0))
            nc.vector.tensor_copy(wc_b[0:NT, :], wc_low[0:NT, :]).then_inc(wc_split, 1)
            dve.wait_ge(dst_in, 48)
            dv = dst_nat[:, :].rearrange("r (c e) -> r c e", e=P)
            nc.vector.tensor_reduce(lo[:, :], dv, AX.X, ALU.min)
            then(nc.vector.tensor_reduce(hi[:, :], dv, AX.X, ALU.max))
            nc.vector.tensor_copy(lo_i[:, :], lo[:, :]).then_inc(lo_set, 1)
            then(nc.vector.tensor_tensor(span[:, :], hi[:, :], lo[:, :], ALU.subtract))
            then(nc.vector.tensor_scalar(wide[:, :], span[:, :], float(WIN), None, ALU.is_ge))
            then(nc.vector.scalar_tensor_tensor(out=shift[:, :], in0=wide[:, :], scalar=-FAR, in1=lo[:, :],
                                                op0=ALU.mult, op1=ALU.add))
            rv = rel_f[:, :].rearrange("r (c e) -> r c e", e=P)
            for q in range(QR):
                cs = slice(q * CQ, (q + 1) * CQ)
                nc.vector.tensor_tensor(rv[:, cs, :], dv[:, cs, :],
                                        shift[:, cs].unsqueeze(2).broadcast_to([NR, CQ, P]),
                                        ALU.subtract).then_inc(rel_set, 1)
            rel_v = rel_t[:, :].rearrange("p (r c) -> p r c", c=CR)
            for q in range(QR):
                dve.wait_ge(rel_tr, q + 1)
                last = nc.vector.tensor_copy(
                    rel_v[:, :, q * CQ:(q + 1) * CQ],
                    rel_banks[q][:, 0:CQ * NR].rearrange("p (c r) -> p r c", c=CQ)).then_inc(rel_out, 1)

            def nodes(i):
                n = sum(chunks_of(i, q) for q in range(QR))
                nc.vector.tensor_tensor(
                    node_1h[:, ds(i * RW, n * WIN)].rearrange("p (c w) -> p c w", w=WIN),
                    iota_w[:, :].unsqueeze(1).broadcast_to([P, n, WIN]),
                    rel_t[:, ds(i * CR, n)].unsqueeze(2).broadcast_to([P, n, WIN]),
                    ALU.is_equal).then_inc(node_hot, 1)

            def hot(i, q):
                if not exists(i, q):
                    return
                n = chunks_of(i, q)
                before, qb = ahead(i, q, -2)
                dve.wait_ge(typ_spread[q], i + 1)
                if exists(before, qb):
                    dve.wait_ge(cf_done[qb], before + 1)
                nc.vector.tensor_scalar(type_1h[:, q % 2, 0:n * P], typ_ps[q % 2][:, 0:n * P], type_p[:, :], None,
                                        ALU.is_equal).then_inc(type_hot[q], 1)

            def spread(i, q):
                if not exists(i, q):
                    return
                n = chunks_of(i, q)
                before, qb = ahead(i, q, -QR)
                dve.wait_ge(cf_done[q], i + 1)
                dve.wait_ge(node_hot, i + 1)
                if exists(before, qb):
                    dve.wait_ge(z_done[q], i)
                nc.vector.tensor_tensor(
                    S[:, q, 0:n * SW].rearrange("p (c b w) -> p c b w", b=NB, w=WIN),
                    node_1h[:, ds(i * RW + q * CQ * WIN, n * WIN)].rearrange("p (c w) -> p c w", w=WIN)
                    .unsqueeze(2).broadcast_to([P, n, NB, WIN]),
                    cf_slot(q)[:, 0:n, :].unsqueeze(3).broadcast_to([P, n, NB, WIN]),
                    ALU.mult).then_inc(s_done[q], 1)

            def edge_round(i, finish):
                for q in range(QR):
                    hot(*ahead(i, q, 3))
                    if q == 1 and not (isinstance(i, int) and i == LAST):
                        nodes(i + 1)
                    spread(*ahead(i, q, 2))
                    if q < 2 and not (isinstance(i, int) and i == 0):
                        add_chunks(i - 1, q * 2 * CQ, (q + 1) * 2 * CQ, i, p_ps)
                    if finish and q == 2:
                        dve_norm(dve, i - LATE)
                if finish:
                    dve_layernorm(dve, i - LATE)
                    dve_out(dve, i - LATE)

            def add_chunks(r, first, end, done_at, window_ps):
                dve.wait_ge(projected, done_at)
                for g in range(first, end, CQ):
                    m = min(CQ, end - g)
                    _, bases = nc.values_load_multi_w_load_instructions(
                        base_row[0:1, ds(r * CR + g, m)], [mybir.EngineType.DVE], min_val=0, max_val=N - 1,
                        skip_runtime_bounds_check_because="a chunk's smallest destination is a node's number")
                    for c in range(m):
                        at = acc[:, ds(bases[c], WIN)]
                        dve.wait_ge(added, r * CR + (g + c))
                        nc.vector.tensor_tensor(at, window_ps[0:D1, (g + c) * WIN:(g + c + 1) * WIN], at,
                                                ALU.add).then_inc(added, 1)

            dve.wait_ge(rel_out, QR)
            nodes(0)
            hot(0, 0)
            hot(0, 1)
            spread(0, 0)
            hot(0, 2)
            spread(0, 1)
            edge_round(0, False)
            then(nc.vector.memset(acc[:, 0:ACC_DVE], 0.0))
            dve.wait_ge(base_in, 16)
            then(nc.vector.tensor_reduce(round_lo[:, :], lo[:, :], AX.X, ALU.min))
            then(nc.vector.tensor_scalar(finished_to[:, :], iota_p[:, :], float(P), -float((LATE - 1) * P), ALU.mult, ALU.add))
            nc.vector.tensor_tensor(odd[:, 0:1], round_lo[:, :], finished_to[0:NR, :], ALU.is_lt)
            nc.vector.tensor_reduce(odd[:, 1:2], wide[:, :], AX.X, ALU.max).then_inc(odd_set, 1)
            dve.wait_ge(odd_sum, 1)
            nc.vector.tensor_scalar(odd_i[:, :], f_ps[0:1, 0:1], 0.0, None, ALU.is_gt).then_inc(odd_out, 1)
            dve.wait_ge(acc_zero_act, 1)
            for i in range(1, LATE + 1):
                edge_round(i, i >= LATE)
            with dve.Fori(LATE + 1, LAST) as i:
                edge_round(i, True)
            edge_round(LAST, True)
            add_chunks(LAST, 0, 2 * CQ, LAST + 1, p_ps)
            add_chunks(LAST, 2 * CQ, CL, LAST + 2, typ_ps[1])
            for k in range(NBLK - LATE, NBLK):
                dve_norm(dve, k)
                dve_layernorm(dve, k)
                dve_out(dve, k)
            redo = dve.value_load(odd_i[0:1, 0:1], min_val=0, max_val=1)
            with dve.If(redo == 1):
                rendezvous(dve, g_hot, g_masked, g_scaled, g_diag, g_added)
                diag = S[:, :, :].rearrange("p q s -> p (q s)")[:, 0:NB * P].rearrange("p (b e) -> p b e", e=P)

                def body(i, j, edges):
                    c = i * CR + j
                    dve.wait_ge(g_spread, c + 2)
                    nc.vector.tensor_scalar(type_1h[:, 0, 0:P], typ_ps[0][:, 0:P], type_p[:, :], None,
                                            ALU.is_equal).then_inc(g_hot, 1)
                    nc.vector.tensor_scalar(g_mask[:, :], rel_t[:, ds(c, 1)], FAR, None, ALU.is_ge).then_inc(g_masked, 1)
                    dve.wait_ge(g_masked, c + 2)
                    dve.wait_ge(g_coef, c + 2)
                    nc.vector.tensor_scalar(g_cf[:, :], cf_ps[0][:, 0:NB], g_mask[:, :], None,
                                            ALU.mult).then_inc(g_scaled, 1)
                    dve.wait_ge(g_scaled, c + 2)
                    nc.vector.tensor_scalar(g_count[:, :], ident[:, :], g_mask[:, :], None, ALU.mult)
                    nc.vector.tensor_tensor(diag, ident[:, :].unsqueeze(1).broadcast_to([P, NB, P]),
                                            g_cf[:, :].unsqueeze(2).broadcast_to([P, NB, P]),
                                            ALU.mult).then_inc(g_diag, 1)
                    dve.wait_ge(g_msg, c + 2)
                    carry_waits(dve)
                    with dve.Fori(0, edges) as e:
                        _, (node,) = nc.values_load_multi_w_load_instructions(
                            dst[ds(c * P + e, 1)].unsqueeze(0), [mybir.EngineType.DVE], min_val=0, max_val=N - 1,
                            skip_runtime_bounds_check_because="a destination is a node's number")
                        at = acc[:, ds(node, 1)]
                        dve.wait_ge(g_added, c * P + e + 1)
                        nc.vector.tensor_tensor(at, f_ps[0:D1, ds(e, 1)], at, ALU.add).then_inc(g_added, 1)

                general(dve, 0, body)
                with dve.Fori(0, NBLK) as k:
                    dve_norm(dve, k + NBLK)
                    dve_layernorm(dve, k + NBLK)
                    dve_out(dve, k + NBLK)

        @block.tensor
        def _(pe):
            pe.wait_ge(pool_const, 4)
            pe.wait_ge(src0_cast, 1)
            nc.tensor.transpose(z_ps[0][:, 0:CR], src0_f[:, :], ident[0:CR, 0:CR]).then_inc(src0_tr, 1)
            for q in range(QR):
                pe.wait_ge(rel_set, q + 1)
                for c in range(CQ):
                    j = q * CQ + c
                    last = nc.tensor.transpose(rel_banks[q][:, c * NR:(c + 1) * NR],
                                               rel_f[:, j * P:(j + 1) * P], ident[0:NR, 0:NR])
                last.then_inc(rel_tr, 1)
            pe.wait_ge(typ_cast, 1)
            pe.wait_ge(ident_cast, 2)
            pe.wait_ge(wc_split, 1)

            def types(i, q):
                if not exists(i, q):
                    return
                n = chunks_of(i, q)
                before, qb = ahead(i, q, -2)
                if exists(before, qb):
                    pe.wait_ge(type_hot[qb], before + 1)
                nc.tensor.matmul(typ_ps[q % 2][:, 0:n * P], ident_b[0:NR, ds(i, 1)].to_broadcast([NR, P]),
                                 typ_b[:, q * CQ * P:(q * CQ + n) * P], start=True, stop=True).then_inc(typ_spread[q], 1)

            def coefs(i, q):
                if not exists(i, q):
                    return
                n = chunks_of(i, q)
                before, qb = ahead(i, q, -QR)
                pe.wait_ge(type_hot[q], i + 1)
                if exists(before, qb):
                    pe.wait_ge(s_done[q], i)
                for c in range(n):
                    one_hot = type_1h[:, q % 2, c * P:(c + 1) * P]
                    nc.tensor.matmul(cf_slot(q)[:, c, :], one_hot, wc_a[:, :], start=True, stop=False)
                    last = nc.tensor.matmul(cf_slot(q)[:, c, :], one_hot, wc_b[:, :], start=False, stop=True)
                last.then_inc(cf_done[q], 1)

            def sums(i, q):
                if not exists(i, q):
                    return
                n = chunks_of(i, q)
                before, qb = ahead(i, q, -2)
                pe.wait_ge(s_done[q], i + 1)
                pe.wait_ge(gathered[q], i * (16 * CQ) + 16 * n)
                if exists(before, qb):
                    pe.wait_ge(z_copied[qb], before + 1)
                for c in range(n):
                    for half in range(2):
                        last = nc.tensor.matmul(z_ps[q % 2][half * D:(half + 1) * D, c * HW:(c + 1) * HW], xg[:, q, c, :],
                                                S[:, q, c * SW + half * HW:c * SW + (half + 1) * HW],
                                                start=True, stop=True)
                last.then_inc(z_done[q], 1)

            def edge_round(i, finish):
                for q in range(QR):
                    types(*ahead(i, q, 3))
                    coefs(*ahead(i, q, 2))
                    if q == 0 and not (isinstance(i, int) and i == 0):
                        project(i - 1, 0, CR, p_ps)
                    if finish and q == 2:
                        pe_xbT(pe, i - LATE)
                    if q == 2 and isinstance(i, int) and i == LAST:
                        project(LAST, 0, 2 * CQ, p_ps)
                    sums(i, q)
                    if finish and q == 2:
                        pe_fin(pe, i - LATE)

            def project(r, first, n, window_ps):
                cols = slice(first * WIN, n * WIN)
                for q in range(first // CQ, -(-n // CQ)):
                    pe.wait_ge(z_copied[q], r + 1)
                if not (isinstance(r, int) and r == 0):
                    pe.wait_ge(added, r * CR)
                for b in range(NH):
                    nc.tensor.matmul(window_ps[0:D1, cols], W[:, b, :], Z[:, b, cols],
                                     start=(b == 0), stop=False)
                pe.wait_ge(node_hot, r + 1)
                whole = n if n < CL or n == CR else EL // P
                last = nc.tensor.matmul(window_ps[0:D1, first * WIN:whole * WIN], count_w[:, :],
                                        node_1h[:, ds(r * RW + first * WIN, (whole - first) * WIN)],
                                        start=False, stop=(whole == n))
                if whole < n:
                    rest = EL - whole * P
                    last = nc.tensor.matmul(window_ps[0:D1, whole * WIN:n * WIN], count_w[0:rest, :],
                                            node_1h[0:rest, r * RW + whole * WIN:r * RW + n * WIN],
                                            start=False, stop=True)
                last.then_inc(projected, 1)

            pe.wait_ge(count_set, 4)
            types(0, 0)
            types(0, 1)
            pe.wait_ge(idx_ready[QR - 1], 1)
            for q in range(QR):
                pe.wait_ge(src_cast, q + 1)
                if q >= 2:
                    pe.wait_ge(src_out, q - 1)
                for c in range(CQ):
                    j = q * CQ + c
                    last = nc.tensor.transpose(z_ps[q % 2][:, c * NR:(c + 1) * NR], src_f[:, j * P:(j + 1) * P],
                                               ident[0:NR, 0:NR])
                last.then_inc(src_tr, 1)
            pe.wait_ge(rel_out, QR)
            coefs(0, 0)
            types(0, 2)
            coefs(0, 1)
            pe.wait_ge(w_in, 80)
            pe.wait_ge(src_out, QR)
            edge_round(0, False)
            pe.wait_ge(odd_set, 1)
            nc.tensor.matmul(f_ps[0:1, 0:1], odd[:, 0:1], ones[0:NR, :], start=True, stop=False)
            nc.tensor.matmul(f_ps[0:1, 0:1], odd[:, 1:2], ones[0:NR, :], start=False, stop=True).then_inc(odd_sum, 1)
            pe.wait_ge(odd_out, 1)
            for i in range(1, LATE + 1):
                edge_round(i, i >= LATE)
            with pe.Fori(LATE + 1, LAST) as i:
                edge_round(i, True)
            edge_round(LAST, True)
            project(LAST, 2 * CQ, CL, typ_ps[1])
            for k in range(NBLK - LATE, NBLK):
                pe_xbT(pe, k)
                pe_fin(pe, k)
            redo = pe.value_load(odd_i[0:1, 0:1], min_val=0, max_val=1)
            with pe.If(redo == 1):
                rendezvous(pe, g_spread, g_coef, g_z, g_msg)
                diag = S[:, :, :].rearrange("p q s -> p (q s)")
                zv = Z[:, :, :].rearrange("p b w -> p (b w)")

                def body(i, j, edges):
                    c = i * CR + j
                    pe.wait_ge(g_hot, c + 1)
                    nc.tensor.matmul(typ_ps[0][:, 0:P], ident_b[0:NR, ds(i, 1)].to_broadcast([NR, P]),
                                     typ_b[:, ds(j * P, P)], start=True, stop=True).then_inc(g_spread, 1)
                    pe.wait_ge(g_hot, c + 2)
                    pe.wait_ge(g_scaled, c + 1)
                    nc.tensor.matmul(cf_ps[0][:, 0:NB], type_1h[:, 0, 0:P], wc_a[:, :], start=True, stop=False)
                    nc.tensor.matmul(cf_ps[0][:, 0:NB], type_1h[:, 0, 0:P], wc_b[:, :], start=False,
                                     stop=True).then_inc(g_coef, 1)
                    pe.wait_ge(g_diag, c + 2)
                    pe.wait_ge(g_gathered, c * 16 + 16)
                    pe.wait_ge(g_zcopied, c + 1)
                    for half in range(2):
                        last = nc.tensor.matmul(z_ps[0][half * D:(half + 1) * D, 0:NH * P], g_x[:, :],
                                                diag[:, half * NH * P:(half + 1) * NH * P], start=True, stop=True)
                    last.then_inc(g_z, 1)
                    pe.wait_ge(g_zcopied, c + 2)
                    pe.wait_ge(g_added, c * P + 1)
                    for b in range(NH):
                        nc.tensor.matmul(f_ps[0:D1, 0:P], W[:, b, :], zv[:, b * P:(b + 1) * P],
                                         start=(b == 0), stop=False)
                    nc.tensor.matmul(f_ps[0:D1, 0:P], count_w[:, :], g_count[:, :],
                                     start=False, stop=True).then_inc(g_msg, 1)

                general(pe, 0, body)
                pe.wait_ge(g_added, E + 1)
                with pe.Fori(0, NBLK) as k:
                    pe_xbT(pe, k + NBLK)
                    pe_fin(pe, k + NBLK)


_INS = ["x", "src", "dst", "edge_type_64", "L0_gnn_weight", "L0_gnn_w_comp", "L0_gnn_loop_weight", "L0_gnn_bias"]


def kernel(**inputs):
    import numpy as np
    import concourse.bacc as bacc
    from concourse.bass_utils import run_bass_kernel_spmd as run

    nc = bacc.Bacc("TRN2", target_bir_lowering=False, num_devices=1)
    arrays, args = {}, []
    for name in _INS:
        a = np.ascontiguousarray(inputs[name])
        arrays[f"in_{name}"] = a
        args.append(nc.dram_tensor(f"in_{name}", a.shape, mybir.dt.from_np(a.dtype), kind="ExternalInput").ap())
    args.append(nc.dram_tensor("out_0", inputs["x"].shape, mybir.dt.float32, kind="ExternalOutput").ap())
    rgcn_kernel(nc, *args)
    return run(nc, [arrays], core_ids=[0]).results[0]["out_0"]
```
